# Optimizing a Trainium2 kernel written in Bass

```python
import numpy as np
import jax
import jax.numpy as jnp

def _softmax(x, axis=-1):
    return jax.nn.softmax(x, axis=axis)

def _gelu(x):
    return jax.nn.gelu(x, approximate=True)

def _silu(x):
    return jax.nn.silu(x)

def _sigmoid(x):
    return jax.nn.sigmoid(x)

def _layernorm(x, axis=-1, eps=1e-05):
    m = jnp.mean(x, axis=axis, keepdims=True)
    v = jnp.var(x, axis=axis, keepdims=True)
    return (x - m) / jnp.sqrt(v + eps)

def _scatter_add(tgt, idx, src, axis=0):
    return tgt.at[idx].add(src)

def _segment_sum(src, seg, n):
    return jax.ops.segment_sum(src, seg, n)
kernel_name = 'mk_early_fusion_d1_tok_img768_r4_cf69c9'

def setup_inputs(seed: int=0):
    np.random.seed(seed)
    _w = jnp.asarray

    def _rec_inputs():
        import jax
        import jax.numpy as jnp
        _rk = jax.random.key(seed)
        x = -0.000356955 + 1 * jax.random.normal(jax.random.fold_in(_rk, 1), (128, 3, 224, 224), jnp.float32)
        txt = -0.000642543 + 1.41352 * jax.random.normal(jax.random.fold_in(_rk, 2), (128, 77, 192), jnp.float32)
        return (x, txt)
    x, txt = _rec_inputs()

    def _L0_tok_setup():
        import jax, jax.numpy as jnp
        import numpy as np
        P = 16
        IMG = 224
        C = 3
        HID = 192
        NP = (IMG // P) ** 2
        PATCH_DIM = C * P * P

        def _extract_patches(images):
            B, c, H, Wd = images.shape
            x = images.reshape(B, c, H // P, P, Wd // P, P)
            x = x.transpose(0, 2, 4, 1, 3, 5)
            return x.reshape(B, H // P * (Wd // P), c * P * P)
        key = jax.random.key(seed)
        k1, k2, k3, k4 = jax.random.split(key, 4)
        images = jax.random.normal(k1, (128, C, IMG, IMG), dtype=jnp.float32)
        W = jax.random.normal(k2, (HID, PATCH_DIM), dtype=jnp.float32) * PATCH_DIM ** (-0.5)
        b = jax.random.normal(k3, (HID,), dtype=jnp.float32) * 0.01
        pos = jax.random.normal(k4, (1, NP, HID), dtype=jnp.float32)
        return {'images': images, 'W': W, 'b': b, 'pos': pos}
    _L0_tok_all = _L0_tok_setup()
    _L0_tok_in = {k: v for k, v in _L0_tok_all.items() if k in ('W', 'b', 'pos')}
    del _L0_tok_all

    def _L0_attn_setup():
        import jax, jax.numpy as jnp
        import numpy as np
        import math
        EMBED_DIM = 192
        NUM_HEADS = 12
        N_QUBITS = 96
        D_K = N_QUBITS // NUM_HEADS
        key = jax.random.key(seed)
        k1, k2, k3 = jax.random.split(key, 3)
        x = jax.random.normal(k1, (8, 256, EMBED_DIM), dtype=jnp.float32)
        theta = jax.random.uniform(k2, (N_QUBITS,), dtype=jnp.float32, minval=-math.pi, maxval=math.pi)
        W_combine = jax.random.normal(k3, (EMBED_DIM, N_QUBITS), dtype=jnp.float32) / math.sqrt(N_QUBITS)
        return {'x': x, 'theta': theta, 'W_combine': W_combine}
    _L0_attn_all = _L0_attn_setup()
    _L0_attn_in = {k: v for k, v in _L0_attn_all.items() if k in ('theta', 'W_combine')}
    del _L0_attn_all

    def _L0_ffn_setup():
        import jax, jax.numpy as jnp
        import numpy as np
        DIM = 192
        HIDDEN = 192
        NUM_EXPERTS = 4
        B, S = (16, 512)
        key = jax.random.key(seed)
        ks = jax.random.split(key, 7)
        sd = 1.0 / np.sqrt(DIM)
        sh = 1.0 / np.sqrt(HIDDEN)
        return {'x': jax.random.normal(ks[0], (B, S, DIM), dtype=jnp.float32), 'router_w': jax.random.uniform(ks[1], (DIM, NUM_EXPERTS), jnp.float32, -sd, sd), 'router_b': jax.random.uniform(ks[2], (NUM_EXPERTS,), jnp.float32, -sd, sd), 'w1': jax.random.uniform(ks[3], (NUM_EXPERTS, DIM, HIDDEN), jnp.float32, -sd, sd), 'b1': jax.random.uniform(ks[4], (NUM_EXPERTS, HIDDEN), jnp.float32, -sd, sd), 'w2': jax.random.uniform(ks[5], (NUM_EXPERTS, HIDDEN, DIM), jnp.float32, -sd, sd), 'b2': jax.random.uniform(ks[6], (NUM_EXPERTS, DIM), jnp.float32, -sd, sd)}
    _L0_ffn_all = _L0_ffn_setup()
    _L0_ffn_in = {k: v for k, v in _L0_ffn_all.items() if k in ('router_w', 'router_b', 'w1', 'b1', 'w2', 'b2')}
    del _L0_ffn_all
    return {'x': x, 'txt': txt, 'L0_tok_W': _L0_tok_in['W'], 'L0_tok_b': _L0_tok_in['b'], 'L0_tok_pos': _L0_tok_in['pos'], 'L0_attn_theta': _L0_attn_in['theta'], 'L0_attn_W_combine': _L0_attn_in['W_combine'], 'L0_ffn_router_w': _L0_ffn_in['router_w'], 'L0_ffn_router_b': _L0_ffn_in['router_b'], 'L0_ffn_w1': _L0_ffn_in['w1'], 'L0_ffn_b1': _L0_ffn_in['b1'], 'L0_ffn_w2': _L0_ffn_in['w2'], 'L0_ffn_b2': _L0_ffn_in['b2']}

def reference(x, txt, L0_tok_W, L0_tok_b, L0_tok_pos, L0_attn_theta, L0_attn_W_combine, L0_ffn_router_w, L0_ffn_router_b, L0_ffn_w1, L0_ffn_b1, L0_ffn_w2, L0_ffn_b2):
    import jax
    import jax.numpy as jnp

    def _L0_tok_ref(images, W, b, pos):
        import jax, jax.numpy as jnp
        import numpy as np
        P = 16
        IMG = 224
        C = 3
        HID = 192
        NP = (IMG // P) ** 2
        PATCH_DIM = C * P * P

        def _extract_patches(images):
            B, c, H, Wd = images.shape
            x = images.reshape(B, c, H // P, P, Wd // P, P)
            x = x.transpose(0, 2, 4, 1, 3, 5)
            return x.reshape(B, H // P * (Wd // P), c * P * P)
        patches = _extract_patches(images)
        emb = jnp.einsum('bnd,hd->bnh', patches, W) + b
        return emb + pos

    def _L0_attn_ref(x, theta, W_combine):
        import jax, jax.numpy as jnp
        import numpy as np
        import math
        EMBED_DIM = 192
        NUM_HEADS = 12
        N_QUBITS = 96
        D_K = N_QUBITS // NUM_HEADS
        B, S, _ = x.shape
        xs = x[..., :N_QUBITS]
        q_vecs = jnp.cos(xs) * jnp.cos(theta)
        q = q_vecs.reshape(B, S, NUM_HEADS, D_K).transpose(0, 2, 1, 3)
        scores = jnp.einsum('bhsd,bhtd->bhst', q, q) / math.sqrt(D_K)
        probs = jax.nn.softmax(scores, axis=-1)
        attn = jnp.einsum('bhst,bhtd->bhsd', probs, q)
        attn = attn.transpose(0, 2, 1, 3).reshape(B, S, N_QUBITS)
        return attn @ W_combine.T

    def _L0_ffn_ref(x, router_w, router_b, w1, b1, w2, b2):
        import jax, jax.numpy as jnp
        import numpy as np
        DIM = 192
        HIDDEN = 192
        NUM_EXPERTS = 4
        B, S = (16, 512)
        logits = jnp.einsum('bsd,de->bse', x, router_w) + router_b
        probs = jax.nn.softmax(logits, axis=-1)
        idx = jnp.argmax(probs, axis=-1)
        dispatch = jax.nn.one_hot(idx, NUM_EXPERTS, dtype=x.dtype)
        h = jnp.einsum('bsd,edh->besh', x, w1) + b1[None, :, None, :]
        h = jax.nn.gelu(h, approximate=False)
        y = jnp.einsum('besh,ehd->besd', h, w2) + b2[None, :, None, :]
        out = jnp.einsum('besd,bse->bsd', y, dispatch)
        out = out + x
        return out
    h = _L0_tok_ref(x, L0_tok_W, L0_tok_b, L0_tok_pos)
    h = jnp.concatenate([h, txt], axis=1)
    h = h + _L0_attn_ref(_layernorm(h, axis=-1), L0_attn_theta, L0_attn_W_combine)
    h = h + _L0_ffn_ref(_layernorm(h, axis=-1), L0_ffn_router_w, L0_ffn_router_b, L0_ffn_w1, L0_ffn_b1, L0_ffn_w2, L0_ffn_b2)
    return h

_drawn_inputs = setup_inputs


def setup_inputs(seed=0):
    import zlib

    import numpy as np

    out = dict(_drawn_inputs(seed))
    spreads = {}
    factors = {'L0_tok_b': 8.0, 'L0_ffn_b1': 8.0, 'L0_ffn_b2': 3.285}
    for name, (base, spread) in spreads.items():
        noise = np.random.default_rng([zlib.crc32(name.encode()), seed]).standard_normal(out[name].shape)
        drawn = base * np.exp(spread * noise) if base else spread * noise
        out[name] = jnp.asarray(drawn.astype(out[name].dtype))
    for name, factor in factors.items():
        out[name] = (out[name] * factor).astype(out[name].dtype)
    return out
```

```python
import numpy as np
import concourse.bass as bass
from concourse import mybir
from contextlib import ExitStack

f32 = mybir.dt.float32
f16 = mybir.dt.float16
ALU = mybir.AluOpType
ACT = mybir.ActivationFunctionType
AX = mybir.AxisListType

B = 128
SLOTS = 2
PAIRS = B // SLOTS
D = 192
TI, TX = 196, 77
T = TI + TX
TS, NT = 98, 3
TP = TS * NT
PD = 768
KP = PD // 128
NQ, NH, DK = 96, 12, 8
NG, HG = 3, 4
KC = 128
KR = T - 2 * KC
TK = 288
NE = 4
HC = NE * D // 128
EPS = 1e-5
TWO_PI = 6.283185307179586
ROUND = 12582912.0
CLOSED = -1e30
UNITS = 2 + NH


class At:

    def __init__(self, base, reg=None):
        self.base, self.reg = base, reg

    def n(self, per, c=0):
        v = per * self.base + c
        return v if self.reg is None else self.reg * per + v

    @property
    def first(self):
        return self.reg is None and self.base == 0

    @property
    def last(self):
        return self.reg is None and self.base == PAIRS - 1

    def next(self):
        return At(self.base + 1, self.reg)

    def prev(self):
        return At(self.base - 1, self.reg)


class Tally:

    def __init__(self, per_loop):
        self.count, self.per_loop, self.reg, self.start = 0, per_loop, None, 0

    def now(self):
        return self.count if self.reg is None else self.reg * self.per_loop + self.count

    def add(self):
        self.count += 1

    def enter(self, reg):
        self.reg, self.start = reg, self.count

    def leave(self, turns):
        assert self.count - self.start == self.per_loop, (self.count - self.start, self.per_loop)
        self.count, self.reg = self.start + turns * self.per_loop, None


def attention_steps(i, s, between):
    for u in range(UNITS):
        yield ("score", i, s, u)
        if u in (8, 12):
            yield ("pv", i, s, (u - 8) // 4)
        if u in (9, 13):
            yield ("norm", i, s, (u - 9) // 4)
        yield from between.get(u, [])


def ffn2_fill(between, g, s, units):
    for p, u in enumerate(units):
        between.setdefault(u, []).append(("ffn2", g, s, p, len(units)))


def pair_steps(i, has_prev, has_next):
    fill = {}
    if has_prev:
        ffn2_fill(fill, i.prev(), 0, range(0, 13))
    yield from attention_steps(i, 0, fill)
    fill = {0: [("pv", i, 0, 2)], 1: [("norm", i, 0, 2)], 2: [("attnT", i, 0)],
            3: [("combine", i, 0), ("ln2_stats", i, 0)], 4: [("ln2_apply", i, 0)],
            5: [("x2T", i, 0)], 6: [("logits", i, 0)], 7: [("hotT", i, 0)]}
    if has_prev:
        ffn2_fill(fill, i.prev(), 1, range(6, 14))
    yield from attention_steps(i, 1, fill)
    g = i.next()
    yield ("pv", i, 1, 2)
    if has_next:
        yield ("txt", g, 0)
        yield ("patch", g, 0, 0)
    yield ("norm", i, 1, 2)
    if has_next:
        yield ("patch", g, 0, 1)
        yield ("ln1_stats", g, 0)
    yield ("attnT", i, 1)
    if has_next:
        yield ("patch", g, 1, 0)
        yield ("ln1_apply", g, 0)
    yield ("combine", i, 1)
    yield ("ln2_stats", i, 1)
    if has_next:
        yield ("txt", g, 1)
        yield ("patch", g, 1, 1)
    yield ("ln2_apply", i, 1)
    if has_next:
        yield ("ln1_stats", g, 1)
    yield ("x2T", i, 1)
    if has_next:
        yield ("ln1_apply", g, 1)
        yield ("cos", g, 0)
        yield ("cos", g, 1)
    yield ("ffn1", i, 0, 0)
    yield ("logits", i, 1)
    yield ("ffn1", i, 0, 1)
    yield ("hotT", i, 1)
    if has_next:
        yield ("q", g, 0)
    yield ("ffn1", i, 0, 2)
    if has_next:
        yield ("q", g, 1)
        yield ("qaT", g, 0)
        yield ("qbT", g, 0)
    yield ("ffn1", i, 1, 0)
    if has_next:
        yield ("qfT", g, 0)
        yield ("qaT", g, 1)
        yield ("vT", g, 0)
    yield ("ffn1", i, 1, 1)
    if has_next:
        yield ("qbT", g, 1)
        yield ("qfT", g, 1)
    yield ("ffn1", i, 1, 2)
    if has_next:
        yield ("vT", g, 1)


def first_steps():
    g = At(0)
    for s in range(SLOTS):
        yield ("txt", g, s)
        yield ("patch", g, s, 0)
        yield ("patch", g, s, 1)
        for step in ("ln1_stats", "ln1_apply", "cos", "q", "qaT", "qbT", "qfT", "vT"):
            yield (step, g, s)


def last_steps():
    g = At(PAIRS - 1)
    for s in range(SLOTS):
        yield ("ffn2", g, s, 0, 1)


def run_steps(eng, mine, tallies):
    def follow(steps):
        for name, i, *where in steps:
            if name in mine:
                mine[name](i, *where)

    follow(first_steps())
    follow(pair_steps(At(0), False, True))
    turns = PAIRS - 2
    with eng.Fori(0, turns) as j:
        for t in tallies:
            t.enter(j)
        follow(pair_steps(At(1, j), True, True))
    for t in tallies:
        t.leave(turns)
    follow(pair_steps(At(PAIRS - 1), True, False))
    follow(last_steps())


def early_fusion_kernel(nc, patches, txt, w_patch, b_patch, pos, theta, w_combine, w_router,
                        b_router, w1, b1, w2, b2, out):
    ctx = ExitStack()
    with ctx:
        def sb(name, shape, dt=f32):
            return ctx.enter_context(nc.sbuf_tensor(name, shape, dt))

        def sem(name):
            return ctx.enter_context(nc.semaphore(name))

        w_patch_sb = sb("w_patch_sb", [128, KP, D])
        pos_sb = sb("pos_sb", [TS, 2, D])
        b_patch_sb = sb("b_patch_sb", [TS, D])
        cos_theta = sb("cos_theta", [TS, NQ])
        w_combine_sb = sb("w_combine_sb", [NQ, D])
        w_router_sb = sb("w_router_sb", [96, 2, NE])
        b_router_sb = sb("b_router_sb", [TS, NE])
        w1_sb = sb("w1_sb", [100, 2, NE * D])
        w2_sb = sb("w2_sb", [128, HC, D])
        b2_sb = sb("b2_sb", [100, D])
        ident = sb("ident", [128, 128])
        ident16 = sb("ident16", [128, 128], f16)
        neg_half = sb("neg_half", [TS, NT])
        half_pi = sb("half_pi", [TS, 1])
        order = sb("order", [TS, NE])
        eps = sb("eps", [TS, NT])
        zero = sb("zero", [TS, 1])
        spare = sb("spare", [1, 1])
        x_sb = sb("x_sb", [128, SLOTS, KP, TI])
        txt_sb = sb("txt_sb", [TS, SLOTS, D])
        h = sb("h", [TS, SLOTS, NT, D])
        stats1 = sb("stats1", [TS, NT, 6])
        moments1 = sb("moments1", [TS, NT, 2])
        rstd1 = sb("rstd1", [TS, SLOTS, NT])
        normed = sb("normed", [TS, NT, NQ])
        turns_sb = sb("turns_sb", [TS, NT, NQ])
        angle = sb("angle", [TS, SLOTS, NT, NQ])
        cos_x = sb("cos_x", [TS, SLOTS, NT, NQ])
        q = sb("q", [TS, SLOTS, NT, NQ])
        q_b = sb("q_b", [TS, SLOTS, NT * NH, 4, DK], f16)
        q_a = sb("q_a", [TS, SLOTS, NT * NH, 4, DK], f16)
        qa_T = sb("qa_T", [128, SLOTS, NG, TK], f16)
        qb_T = sb("qb_T", [128, SLOTS, NG, TK], f16)
        qa_rest = sb("qa_rest", [128, SLOTS, NG, 128], f16)
        q_T = sb("q_T", [NQ, SLOTS, 2 * KC + HG * 32])
        v = sb("v", [128, SLOTS, 2, NH, DK + 1])
        v_rest = sb("v_rest", [128, SLOTS, NG, 128])
        probs = sb("probs", [128, 2, HG, 2, T])
        probs_rest = sb("probs_rest", [128, SLOTS, NG, T])
        o_T = sb("o_T", [128, 2, TP])
        recip = sb("recip", [TS, NT * HG])
        attn = sb("attn", [TS, SLOTS, NT, NQ])
        attn_T = sb("attn_T", [NQ, TP])
        h1 = sb("h1", [TS, SLOTS, NT, D])
        stats2 = sb("stats2", [TS, NT, 6])
        moments2 = sb("moments2", [TS, NT, 2])
        rstd2 = sb("rstd2", [TS, SLOTS, NT])
        x2 = sb("x2", [TS, SLOTS, NT, D])
        resid = sb("resid", [TS, SLOTS, NT, D])
        x2_T = sb("x2_T", [100, 2, SLOTS, TP])
        logit = sb("logit", [TS, NT, NE])
        top = sb("top", [TS, NT])
        ranked = sb("ranked", [TS, NT, NE])
        best = sb("best", [TS, NT])
        onehot = sb("onehot", [TS, NT, 100])
        hidden = sb("hidden", [128, HC, SLOTS, TP])
        o_sb = sb("o_sb", [TS, SLOTS, NT, D])

        pair_ps = [ctx.enter_context(nc.psum_tensor(f"pair_ps{n}", [128, 2, 512], f32)) for n in (0, 1)]
        bank4 = ctx.enter_context(nc.psum_tensor("bank4", [128, 512], f32))
        wide = ctx.enter_context(nc.psum_tensor("wide", [128, 1024], f32))
        narrow = ctx.enter_context(nc.psum_tensor("narrow", [128, 512], f32))
        narrow16 = narrow[:, :].bitcast(f16)

        consts_loaded = sem("consts_loaded")
        consts_made = sem("consts_made")
        theta_cos = sem("theta_cos")
        consts_ready = sem("consts_ready")
        x_loaded = [sem(f"x_loaded{s}") for s in range(SLOTS)]
        txt_loaded = [sem(f"txt_loaded{s}") for s in range(SLOTS)]
        stored = [sem(f"stored{s}") for s in range(SLOTS)]
        patch_done, patch_read = sem("patch_done"), sem("patch_read")
        txt_placed = sem("txt_placed")
        ln1_stats, ln1_rstd, angle_ready, cos_ready = (
            sem("ln1_stats"), sem("ln1_rstd"), sem("angle_ready"), sem("cos_ready"))
        q_split, qa_ready = sem("q_split"), sem("qa_ready")
        scores_done, exp_done = sem("scores_done"), sem("exp_done")
        pv_done, pv_read = sem("pv_done"), sem("pv_read")
        narrow_done, narrow_read = sem("narrow_done"), sem("narrow_read")
        combine_done, h1_ready = sem("combine_done"), sem("h1_ready")
        ln2_stats, ln2_rstd, x2_ready, resid_ready = (
            sem("ln2_stats"), sem("ln2_rstd"), sem("x2_ready"), sem("resid_ready"))
        x2T_done, x2T_ready = sem("x2T_done"), sem("x2T_ready")
        hot_ready = sem("hot_ready")
        ffn1_done, gelu_done = sem("ffn1_done"), sem("gelu_done")
        ffn2_done, o_ready = sem("ffn2_done"), sem("o_ready")
        dve_chain, pool_chain = sem("dve_chain"), sem("pool_chain")

        NARROW_PER_PAIR = SLOTS * (NG + 3 + 4)
        N_CONST_DMAS = 11 + NE
        N_MADE = 26

        block = ctx.enter_context(nc.Block())

        @block.sync
        def _(sp):
            for dst, src in ((w_patch_sb[:], w_patch), (pos_sb[:], pos),
                             (b_patch_sb[:], b_patch.partition_broadcast(TS)),
                             (normed[:, 0, :], theta.partition_broadcast(TS)),
                             (w_combine_sb[:], w_combine), (w_router_sb[:], w_router),
                             (b_router_sb[:], b_router.partition_broadcast(TS)),
                             (w1_sb[0:96, 0, :], w1[0]), (w1_sb[0:96, 1, :], w1[1]),
                             (w2_sb[:], w2), (b2_sb[96:100, :], b2)):
                sp.dma_start(dst, src).then_inc(consts_loaded, 16)

            def load(i, s):
                b = i.n(SLOTS, s)
                if not i.first:
                    sp.wait_ge(ln1_stats, i.n(2, s - 1))
                sp.dma_start(x_sb[:, s], patches[b]).then_inc(x_loaded[s], 16)
                sp.dma_start(txt_sb[0:TX, s, :], txt[b]).then_inc(txt_loaded[s], 16)

            def store(i, s, part, parts):
                if part != parts - 1:
                    return
                b = i.n(SLOTS, s)
                sp.wait_ge(o_ready, i.n(2, s + 1))
                sp.dma_start(out[b, 0:TI].rearrange("(t p) d -> p t d", p=TS),
                             o_sb[:, s, 0:2, :]).then_inc(stored[s], 16)
                sp.dma_start(out[b, TI:T], o_sb[0:TX, s, 2, :]).then_inc(stored[s], 16)

            sp.wait_ge(consts_made, N_MADE)
            for e in range(NE):
                sp.dma_start(w1_sb[96 + e:97 + e, 1, e * D:(e + 1) * D], b1[e:e + 1, :]).then_inc(consts_loaded, 16)
            for s in range(SLOTS):
                load(At(0), s)
            def load_next(i, s, u):
                if u == 0 and not i.last:
                    load(i.next(), s)

            run_steps(sp, {"score": load_next, "ffn2": store}, [])
            for s in range(SLOTS):
                sp.wait_ge(stored[s], 32 * PAIRS)

        @block.gpsimd
        def _(pool):
            made = [0]

            def make(ins):
                made[0] += 1
                ins.then_inc(consts_made, 1)
                pool.wait_ge(consts_made, made[0])

            make(pool.memset(ident[:], 0.0))
            make(pool.memset(ident16[:], 0.0))
            make(pool.memset(neg_half[:], -0.5))
            make(pool.memset(half_pi[:], TWO_PI / 4))
            make(pool.memset(eps[:], EPS))
            make(pool.memset(zero[:], 0.0))
            for e in range(NE):
                make(pool.memset(order[:, e:e + 1], float(NE - e)))
            make(pool.memset(txt_sb[:], 0.0))
            make(pool.memset(w1_sb[96:100, 1, :], CLOSED))
            make(pool.memset(qa_T[:], 0.0))
            make(pool.memset(qa_rest[:], 0.0))
            make(pool.memset(q_T[:], 0.0))
            make(pool.memset(v[:], 1.0))
            make(pool.memset(v_rest[:], 0.0))
            make(pool.memset(o_T[:], 1.0))
            make(pool.memset(onehot[:], 0.0))
            make(pool.memset(hidden[:], 0.0))
            for m in (ident, ident16):
                make(pool.affine_select(out=m[:], in_=m[:], compare_op=ALU.not_equal, fill=1.0, base=0,
                                        pattern=[[-1, 128]], channel_multiplier=1))
            for g in range(HG):
                for s in range(1):
                    make(pool.memset(v_rest[32 * g:32 * g + KR, :, :, 32 * g + DK:32 * g + DK + 1], 1.0))
            assert made[0] == N_MADE, made

            chain = Tally(2 * SLOTS)

            def link(ins):
                chain.add()
                ins.then_inc(pool_chain, 1)
                pool.wait_ge(pool_chain, chain.now())

            def place_text(i, s):
                pool.wait_ge(txt_loaded[s], i.n(16, 16))
                if not i.first:
                    pool.wait_ge(h1_ready, i.n(2, s - 1))
                pool.tensor_tensor(h[:, s, 2, :], txt_sb[:, s, :], zero[:].to_broadcast([TS, D]), ALU.add).then_inc(txt_placed, 1)

            def inverse_deviation(rstd, moments, done, stats, i, s):
                pool.wait_ge(stats, i.n(2, s + 1))
                link(pool.tensor_tensor(rstd[:, s, :], moments[:, :, 1], eps[:], ALU.add))
                pool.tensor_tensor(rstd[:, s, :], rstd[:, s, :], neg_half[:], ALU.pow).then_inc(done, 1)

            def rstd_1(i, s):
                inverse_deviation(rstd1, moments1, ln1_rstd, ln1_stats, i, s)

            def rstd_2(i, s):
                inverse_deviation(rstd2, moments2, ln2_rstd, ln2_stats, i, s)

            def copy_parts(i, s):
                pool.wait_ge(q_split, i.n(2, s + 1))
                pool.tensor_tensor(q_a[:, s, :, 0, :], q_b[:, s, :, 0, :],
                                   zero[:, :, None].to_broadcast([TS, NT * NH, DK]), ALU.add)
                for part in range(1, 4):
                    ins = pool.tensor_copy(q_a[:, s, :, part, :], q_b[:, s, :, part // 2, :])
                ins.then_inc(qa_ready, 1)

            def residual(i, s):
                pool.wait_ge(x2_ready, i.n(2, s + 1))
                pool.tensor_tensor(resid[:, s], h1[:, s], x2[:, s], ALU.add).then_inc(resid_ready, 1)

            run_steps(pool, {"txt": place_text, "ln1_stats": rstd_1, "ln2_stats": rstd_2,
                             "q": copy_parts, "ln2_apply": residual}, [chain])

        @block.scalar
        def _(act):
            act.wait_ge(consts_made, N_MADE)
            act.wait_ge(theta_cos, 1)
            act.activation(cos_theta[:], cos_x[:, 0, 0, :], ACT.Sin, bias=half_pi[:, 0:1],
                           scale=-1.0).then_inc(theta_cos, 1)

            def cosine(i, s):
                act.wait_ge(angle_ready, i.n(2, s + 1))
                act.activation(cos_x[:, s], angle[:, s], ACT.Sin, bias=half_pi[:, 0:1],
                               scale=-1.0).then_inc(cos_ready, 1)

            def exponential(i, s, u):
                n = s * UNITS + u
                act.wait_ge(scores_done, i.n(2 * UNITS, n + 1))
                if u == 0 and not i.first:
                    act.wait_ge(pv_done, i.n(2 * NG, NG * (s - 1)))
                group = NG * s + (u - 2) // HG
                if u >= 2 and (u - 2) % HG == 0 and not (i.first and group < 2):
                    act.wait_ge(pv_done, i.n(2 * NG, group - 1))
                src = pair_ps[n % 2]
                if u == 0:
                    a, b = probs_rest[:, s, 0:2, :], src[:, :, 0:T]
                elif u == 1:
                    a, b = probs_rest[:, s, 2, :], src[:, 0, 0:T]
                else:
                    j, g = divmod(u - 2, HG)
                    a, b = probs[:, (NG * s + j) % 2, g], src[:, :, 0:T]
                act.activation(a, b, ACT.Exp, scale=DK ** -0.5).then_inc(exp_done, 1)

            def gelu(i, s, c):
                act.wait_ge(ffn1_done, i.n(6, 3 * s + c + 1))
                act.activation(hidden[:, 2 * c:2 * c + 2, s, 0:T], pair_ps[(3 * s + c) % 2][:, :, 0:T],
                               ACT.Gelu).then_inc(gelu_done, 1)

            run_steps(act, {"cos": cosine, "score": exponential, "ffn1": gelu}, [])

        @block.vector
        def _(dve):
            chain = Tally(16 * SLOTS)
            jobs = Tally(NARROW_PER_PAIR)

            def link(ins):
                chain.add()
                ins.then_inc(dve_chain, 1)
                dve.wait_ge(dve_chain, chain.now())

            def narrow_result():
                jobs.add()
                dve.wait_ge(narrow_done, jobs.now())

            def reduce_angle(out, x, tmp, exact_turns):
                link(dve.tensor_scalar(tmp, x, 1 / TWO_PI, ROUND, ALU.mult, ALU.add))
                if exact_turns:
                    link(dve.tensor_scalar(tmp, tmp, ROUND, -TWO_PI, ALU.subtract, ALU.mult))
                    link(dve.tensor_tensor(tmp, tmp, x, ALU.add))
                else:
                    link(dve.tensor_scalar(out, tmp, ROUND, -6.28125, ALU.subtract, ALU.mult))
                    link(dve.tensor_tensor(x, out, x, ALU.add))
                    link(dve.tensor_scalar(tmp, tmp, ROUND, 6.28125 - TWO_PI, ALU.subtract, ALU.mult))
                    link(dve.tensor_tensor(tmp, tmp, x, ALU.add))
                return dve.scalar_tensor_tensor(out, tmp, -1.0, tmp, ALU.mult, ALU.max)

            dve.wait_ge(consts_loaded, 16 * N_CONST_DMAS)
            dve.tensor_tensor(pos_sb[:], pos_sb[:], b_patch_sb[:, None, :].to_broadcast([TS, 2, D]),
                              ALU.add).then_inc(consts_ready, 1)
            reduce_angle(cos_x[:, 0, 0, :], normed[:, 0, :], turns_sb[:, 0, :], False).then_inc(theta_cos, 1)
            dve.wait_ge(theta_cos, 2)
            dve.wait_ge(consts_made, N_MADE)
            dve.wait_ge(consts_ready, 1)

            def embed(i, s, t):
                if t == 1:
                    dve.wait_ge(patch_done, i.n(2, s + 1))
                    src = bank4[0:TS, :].rearrange("p (t c) -> p t c", t=2)[:, :, 0:D]
                    dve.tensor_tensor(h[:, s, 0:2, :], src, pos_sb[:], ALU.add).then_inc(patch_read, 1)

            def moments(x, stats, mom, done):
                for t in range(NT):
                    ins = dve.bn_stats(stats[:, t, :], x[:, t, :])
                link(ins)
                dve.memset(spare[:], 0.0)
                for t in range(NT):
                    ins = dve.bn_aggr(mom[:, t, :], stats[:, t, :])
                ins.then_inc(done, 1)

            def moments_1(i, s):
                dve.wait_ge(patch_read, i.n(2, s + 1))
                dve.wait_ge(txt_placed, i.n(2, s + 1))
                moments(h[:, s], stats1, moments1, ln1_stats)

            def angles(i, s):
                dve.wait_ge(ln1_rstd, i.n(2, s + 1))
                for t in range(NT):
                    ins = dve.tensor_scalar(normed[:, t, :], h[:, s, t, 0:NQ], moments1[:, t, 0:1],
                                            rstd1[:, s, t:t + 1], ALU.subtract, ALU.mult)
                link(ins)
                reduce_angle(angle[:, s], normed[:], turns_sb[:], True).then_inc(angle_ready, 1)

            def split_q(i, s):
                dve.wait_ge(cos_ready, i.n(2, s + 1))
                link(dve.tensor_tensor(q[:, s], cos_x[:, s], cos_theta[:, None, :].to_broadcast([TS, NT, NQ]), ALU.mult))
                qv = q[:, s].rearrange("p t (h d) -> p (t h) d", d=DK)
                link(dve.tensor_copy(q_b[:, s, :, 0, :], qv))
                dve.tensor_copy(q_b[:, s, :, 2, :], qv)
                dve.tensor_tensor(q_b[:, s, :, 1, :], qv, q_b[:, s, :, 0, :], ALU.subtract)
                dve.tensor_tensor(q_b[:, s, :, 3, :], qv, q_b[:, s, :, 0, :], ALU.subtract).then_inc(q_split, 1)

            def parts_T(dst):
                src = narrow16[:, 0:NG * TP].rearrange("p (j t) -> p j t", j=NG)[:, :, 0:T]
                return dve.tensor_copy(dst, src)

            def read_qaT(i, s):
                narrow_result()
                parts_T(qa_T[:, s, :, 0:T])
                for g in range(HG):
                    src = narrow16[32 * g:32 * g + 32, 0:NG * TP].rearrange("p (j t) -> p j t", j=NG)
                    ins = dve.tensor_copy(qa_rest[32 * g:32 * g + 32, s, :, 32 * g:32 * g + KR], src[:, :, 2 * KC:T])
                ins.then_inc(narrow_read, 1)

            def read_qbT(i, s):
                narrow_result()
                parts_T(qb_T[:, s, :, 0:T]).then_inc(narrow_read, 1)

            def read_qfT(i, s):
                narrow_result()
                dve.tensor_copy(q_T[:, s, 0:2 * KC], narrow[0:NQ, 0:2 * KC])
                dve.tensor_copy(q_T[:, s, 2 * KC:].rearrange("p (g t) -> p g t", g=HG)[:, :, 0:KR],
                                narrow[0:NQ, 2 * KC:T][:, None, :].to_broadcast([NQ, HG, KR])).then_inc(narrow_read, 1)

            def read_vT(i, s):
                narrow_result()
                dve.tensor_copy(v[:, s, :, :, 0:DK].rearrange("p c h d -> p (c h) d"),
                                narrow[:, 0:2 * NQ].rearrange("p (x d) -> p x d", d=DK))
                for g in range(HG):
                    src = narrow[32 * g:32 * g + 32, 2 * NQ:3 * NQ].rearrange("p (j x) -> p j x", j=NG)
                    ins = dve.tensor_copy(v_rest[32 * g:32 * g + 32, s, :, 32 * g:32 * g + DK],
                                          src[:, :, DK * g:DK * g + DK])
                ins.then_inc(narrow_read, 1)

            def read_pv(i, s, j):
                n = NG * s + j
                dve.wait_ge(pv_done, i.n(2 * NG, n + 1))
                dve.tensor_copy(o_T[:, n % 2, 0:T], bank4[:, 0:T]).then_inc(pv_read, 1)

            def normalise(i, s, j):
                narrow_result()
                src = narrow[0:TS, 0:NT * 128].rearrange("p (t g x) -> p t g x", t=NT, g=HG)
                link(dve.reciprocal(recip[:], src[:, :, :, DK].rearrange("p t g -> p (t g)")))
                dst = attn[:, s, :, 32 * j:32 * j + 32].rearrange("p t (g d) -> p t g d", d=DK)
                rv = recip[:].rearrange("p (t g) -> p t g", t=NT)[:, :, :, None].to_broadcast([TS, NT, HG, DK])
                dve.tensor_tensor(dst, src[:, :, :, 0:DK], rv, ALU.mult).then_inc(narrow_read, 1)

            def read_attnT(i, s):
                narrow_result()
                dve.tensor_copy(attn_T[:], narrow[0:NQ, 0:TP]).then_inc(narrow_read, 1)

            wide_tiles = wide[0:TS, :].rearrange("p (t c) -> p t c", t=4)[:, 0:NT, 0:D]

            def add_attention(i, s):
                dve.wait_ge(combine_done, i.n(2, s + 1))
                dve.tensor_tensor(h1[:, s], wide_tiles, h[:, s], ALU.add).then_inc(h1_ready, 1)

            def moments_2(i, s):
                dve.wait_ge(h1_ready, i.n(2, s + 1))
                moments(h1[:, s], stats2, moments2, ln2_stats)

            def norm_2(i, s):
                dve.wait_ge(ln2_rstd, i.n(2, s + 1))
                for t in range(NT):
                    ins = dve.tensor_scalar(x2[:, s, t, :], h1[:, s, t, :], moments2[:, t, 0:1],
                                            rstd2[:, s, t:t + 1], ALU.subtract, ALU.mult)
                ins.then_inc(x2_ready, 1)

            def read_x2T(i, s):
                dve.wait_ge(x2T_done, i.n(2, s + 1))
                dve.tensor_copy(x2_T[0:96, :, s, :],
                                wide[0:96, :].rearrange("p (c t) -> p c t", c=2)[:, :, 0:TP]).then_inc(x2T_ready, 1)

            def choose(i, s):
                narrow_result()
                src = narrow[0:TS, 0:NT * NE].rearrange("p (t e) -> p t e", e=NE)
                link(dve.tensor_tensor(logit[:], src, b_router_sb[:, None, :].to_broadcast([TS, NT, NE]), ALU.add))
                link(dve.tensor_reduce(top[:], logit[:], AX.X, ALU.max))
                link(dve.tensor_tensor(ranked[:], logit[:], top[:, :, None].to_broadcast([TS, NT, NE]), ALU.is_equal))
                link(dve.tensor_tensor(ranked[:], ranked[:], order[:, None, :].to_broadcast([TS, NT, NE]), ALU.mult))
                link(dve.tensor_reduce(best[:], ranked[:], AX.X, ALU.max))
                dve.tensor_tensor(onehot[:, :, 96:100], ranked[:], best[:, :, None].to_broadcast([TS, NT, NE]),
                                  ALU.is_equal).then_inc(narrow_read, 1)

            def read_hotT(i, s):
                narrow_result()
                dve.tensor_copy(x2_T[96:100, 1, s, :], narrow[96:100, 0:TP]).then_inc(narrow_read, 1)

            def finish(i, s, part, parts):
                if part != parts - 1:
                    return
                dve.wait_ge(ffn2_done, i.n(2, s + 1))
                dve.wait_ge(resid_ready, i.n(2, s + 1))
                if not i.first:
                    dve.wait_ge(stored[s], i.n(32))
                dve.tensor_tensor(o_sb[:, s], wide_tiles, resid[:, s], ALU.add).then_inc(o_ready, 1)

            run_steps(dve, {"patch": embed, "ln1_stats": moments_1, "ln1_apply": angles, "q": split_q,
                            "qaT": read_qaT, "qbT": read_qbT, "qfT": read_qfT, "vT": read_vT,
                            "pv": read_pv, "norm": normalise, "attnT": read_attnT,
                            "combine": add_attention, "ln2_stats": moments_2, "ln2_apply": norm_2,
                            "x2T": read_x2T, "logits": choose, "hotT": read_hotT, "ffn2": finish},
                      [chain, jobs])

        @block.tensor
        def _(pe):
            pe.wait_ge(consts_made, N_MADE)
            pe.wait_ge(consts_loaded, 16 * N_CONST_DMAS)
            jobs = Tally(NARROW_PER_PAIR)

            def narrow_free():
                if jobs.reg is not None or jobs.count:
                    pe.wait_ge(narrow_read, jobs.now())
                jobs.add()

            def patch(i, s, t):
                if t == 0:
                    pe.wait_ge(x_loaded[s], i.n(16, 16))
                    if s == 1:
                        pe.wait_ge(patch_read, i.n(2, 1))
                    elif not i.first:
                        pe.wait_ge(pv_read, i.n(2 * NG))
                for k in range(KP):
                    ins = pe.matmul(bank4[0:TS, 256 * t:256 * t + D], x_sb[:, s, k, TS * t:TS * t + TS],
                                    w_patch_sb[:, k, :], start=k == 0, stop=k == KP - 1)
                if t == 1:
                    ins.then_inc(patch_done, 1)

            def parts_T(src, s):
                for j in range(NG):
                    for t in range(NT):
                        at = t * NH + HG * j
                        ins = pe.transpose(narrow16[:, j * TP + t * TS:j * TP + (t + 1) * TS],
                                           src[:, s, at:at + HG].rearrange("p h x d -> p (h x d)"),
                                           ident16[0:TS, 0:TS])
                ins.then_inc(narrow_done, 1)

            def qaT(i, s):
                pe.wait_ge(qa_ready, i.n(2, s + 1))
                narrow_free()
                parts_T(q_a, s)

            def qbT(i, s):
                pe.wait_ge(q_split, i.n(2, s + 1))
                narrow_free()
                parts_T(q_b, s)

            def qfT(i, s):
                narrow_free()
                for t in range(NT):
                    ins = pe.transpose(narrow[0:NQ, TS * t:TS * t + TS], q[:, s, t, :], ident[0:TS, 0:TS])
                ins.then_inc(narrow_done, 1)

            def vT(i, s):
                narrow_free()
                for c in range(2):
                    pe.transpose(narrow[:, NQ * c:NQ * c + NQ], q_T[:, s, KC * c:KC * c + KC], ident[0:NQ, 0:NQ])
                pe.transpose(narrow[:, 2 * NQ:3 * NQ], q_T[:, s, 2 * KC:], ident[0:NQ, 0:NQ]).then_inc(narrow_done, 1)

            def score(i, s, u):
                n = s * UNITS + u
                if u == 0:
                    pe.wait_ge(narrow_read, jobs.now())
                if n >= 2:
                    pe.wait_ge(exp_done, i.n(2 * UNITS, n - 1))
                elif not i.first:
                    pe.wait_ge(gelu_done, i.n(6, n - 1))
                dst = pair_ps[n % 2]
                if u < 2:
                    for x, j in enumerate((0, 1) if u == 0 else (2,)):
                        ins = pe.matmul(dst[:, x, 0:T], qa_rest[:, s, j, :], qb_T[:, s, j, 0:T], start=True, stop=True)
                else:
                    j, g = divmod(u - 2, HG)
                    for c in range(2):
                        ins = pe.matmul(dst[:, c, 0:T], qa_T[32 * g:32 * g + 32, s, j, KC * c:KC * c + KC],
                                        qb_T[32 * g:32 * g + 32, s, j, 0:T], start=True, stop=True)
                ins.then_inc(scores_done, 1)

            def pv(i, s, j):
                n = NG * s + j
                pe.wait_ge(exp_done, i.n(2 * UNITS, UNITS * s + 2 + HG * (j + 1)))
                if n == 0:
                    pe.wait_ge(patch_read, i.n(2, 2))
                else:
                    pe.wait_ge(pv_read, i.n(2 * NG, n))
                pe.matmul(bank4[:, 0:T], v_rest[:, s, j, :], probs_rest[:, s, j, :], start=True, stop=False)
                for c in range(2):
                    for g in range(HG):
                        ins = pe.matmul(bank4[32 * g:32 * g + DK + 1, 0:T], v[:, s, c, HG * j + g, :],
                                        probs[:, n % 2, g, c, :], start=False, stop=c == 1)
                ins.then_inc(pv_done, 1)

            def norm(i, s, j):
                pe.wait_ge(pv_read, i.n(2 * NG, NG * s + j + 1))
                narrow_free()
                for t in range(NT):
                    ins = pe.transpose(narrow[0:TS, 128 * t:128 * t + 128],
                                       o_T[:, (NG * s + j) % 2, TS * t:TS * t + TS], ident[:])
                ins.then_inc(narrow_done, 1)

            def attnT(i, s):
                narrow_free()
                for t in range(NT):
                    ins = pe.transpose(narrow[0:NQ, TS * t:TS * t + TS], attn[:, s, t, :], ident[0:TS, 0:TS])
                ins.then_inc(narrow_done, 1)

            def combine(i, s):
                pe.wait_ge(narrow_read, jobs.now())
                if not i.first:
                    pe.wait_ge(o_ready, i.n(2, s - 1))
                elif s == 1:
                    pe.wait_ge(x2T_ready, 1)
                for t in range(NT):
                    ins = pe.matmul(wide[0:TS, 256 * t:256 * t + D], attn_T[:, TS * t:TS * t + TS],
                                    w_combine_sb[:], start=True, stop=True)
                ins.then_inc(combine_done, 1)

            def x2T(i, s):
                pe.wait_ge(x2_ready, i.n(2, s + 1))
                for c in range(2):
                    for t in range(NT):
                        ins = pe.transpose(wide[0:96, 512 * c + TS * t:512 * c + TS * t + TS],
                                           x2[:, s, t, 96 * c:96 * c + 96], ident[0:TS, 0:TS])
                ins.then_inc(x2T_done, 1)

            def logits(i, s):
                pe.wait_ge(x2T_ready, i.n(2, s + 1))
                narrow_free()
                for t in range(NT):
                    for c in range(2):
                        ins = pe.matmul(narrow[0:TS, NE * t:NE * t + NE], x2_T[0:96, c, s, TS * t:TS * t + TS],
                                        w_router_sb[:, c, :], start=c == 0, stop=c == 1)
                ins.then_inc(narrow_done, 1)

            hot_at = [None, None]

            def hotT(i, s):
                narrow_free()
                for t in range(NT):
                    ins = pe.transpose(narrow[0:100, TS * t:TS * t + TS], onehot[:, t, :], ident[0:TS, 0:TS])
                ins.then_inc(narrow_done, 1)
                hot_at[s] = jobs.now()

            def ffn1(i, s, c):
                n = 3 * s + c
                if c == 0:
                    pe.wait_ge(narrow_read, hot_at[s])
                if n < 2:
                    pe.wait_ge(exp_done, i.n(2 * UNITS, 2 * UNITS - 1 + n))
                else:
                    pe.wait_ge(gelu_done, i.n(6, n - 1))
                for x in range(2):
                    m = 128 * (2 * c + x)
                    pe.matmul(pair_ps[n % 2][:, x, 0:T], w1_sb[0:96, 0, m:m + 128], x2_T[0:96, 0, s, 0:T],
                              start=True, stop=False)
                    ins = pe.matmul(pair_ps[n % 2][:, x, 0:T], w1_sb[0:100, 1, m:m + 128], x2_T[0:100, 1, s, 0:T],
                                    start=False, stop=True)
                ins.then_inc(ffn1_done, 1)

            def ffn2(i, s, part, parts):
                total = NT * (HC + 1)
                if part == 0:
                    pe.wait_ge(gelu_done, i.n(6, 3 * s + 3))
                    if parts == 1 and s == 1:
                        pe.wait_ge(o_ready, i.n(2, 1))
                    else:
                        pe.wait_ge(x2T_ready, i.n(2, 2 + s))
                for k in range(part * total // parts, (part + 1) * total // parts):
                    t, m = divmod(k, HC + 1)
                    dst = wide[0:TS, 256 * t:256 * t + D]
                    tok = slice(TS * t, TS * t + TS)
                    if m < HC:
                        ins = pe.matmul(dst, hidden[:, m, s, tok], w2_sb[:, m, :], start=m == 0, stop=False)
                    else:
                        ins = pe.matmul(dst, x2_T[96:100, 1, s, tok], b2_sb[96:100, :], start=False, stop=True)
                if part == parts - 1:
                    ins.then_inc(ffn2_done, 1)

            run_steps(pe, {"patch": patch, "qaT": qaT, "qbT": qbT, "qfT": qfT, "vT": vT, "score": score,
                           "pv": pv, "norm": norm, "attnT": attnT, "combine": combine, "x2T": x2T,
                           "logits": logits, "hotT": hotT, "ffn1": ffn1, "ffn2": ffn2}, [jobs])


def kernel(x, txt, L0_tok_W, L0_tok_b, L0_tok_pos, L0_attn_theta, L0_attn_W_combine, L0_ffn_router_w,
           L0_ffn_router_b, L0_ffn_w1, L0_ffn_b1, L0_ffn_w2, L0_ffn_b2):
    import concourse.bacc as bacc
    from concourse.bass_utils import run_bass_kernel_spmd

    x = np.asarray(x)
    side = x.shape[-1] // 16
    patches = x.reshape(B, 3, side, 16, side, 16).transpose(0, 1, 3, 5, 2, 4).reshape(B, KP, 128, TI)
    arrays = {
        "patches": patches.transpose(0, 2, 1, 3),
        "txt": np.asarray(txt),
        "w_patch": np.asarray(L0_tok_W).T.reshape(KP, 128, D).transpose(1, 0, 2),
        "b_patch": np.asarray(L0_tok_b),
        "pos": np.asarray(L0_tok_pos).reshape(2, TS, D).transpose(1, 0, 2),
        "theta": np.asarray(L0_attn_theta),
        "w_combine": np.asarray(L0_attn_W_combine).T,
        "w_router": np.asarray(L0_ffn_router_w).reshape(2, 96, NE).transpose(1, 0, 2),
        "b_router": np.asarray(L0_ffn_router_b),
        "w1": np.asarray(L0_ffn_w1).transpose(1, 0, 2).reshape(2, 96, NE * D),
        "b1": np.asarray(L0_ffn_b1),
        "w2": np.asarray(L0_ffn_w2).reshape(HC, 128, D).transpose(1, 0, 2),
        "b2": np.asarray(L0_ffn_b2),
    }
    arrays = {k: np.ascontiguousarray(a) for k, a in arrays.items()}
    nc = bacc.Bacc("TRN2", target_bir_lowering=False, num_devices=1)
    aps = {k: nc.dram_tensor(k, a.shape, f32, kind="ExternalInput").ap() for k, a in arrays.items()}
    out = nc.dram_tensor("out", (B, T, D), f32, kind="ExternalOutput").ap()
    early_fusion_kernel(nc, out=out, **aps)
    r = run_bass_kernel_spmd(nc, [arrays], core_ids=[0])
    return r.results[0]["out"]
```

```python
import numpy as np
import concourse.bass as bass
from concourse import mybir
from contextlib import ExitStack

f32 = mybir.dt.float32
f16 = mybir.dt.float16
bf16 = mybir.dt.bfloat16
ALU = mybir.AluOpType
ACT = mybir.ActivationFunctionType
AX = mybir.AxisListType

B = 128
SLOTS = 2
PAIRS = B // SLOTS
D = 192
TI, TX = 196, 77
T = TI + TX
TS, NT = 98, 3
TP = TS * NT
PD = 768
KP = PD // 128
NQ, NH, DK = 96, 12, 8
NG, HG = 3, 4
KC = 128
KR = T - 2 * KC
TK = 288
NE = 4
PARTS = 3
RC = 80
HOT = 32 * (PARTS - 1) + NE
HC = NE * D // 128
EPS = 1e-5
TWO_PI = 6.283185307179586
ROUND = 12582912.0
CLOSED = -1e30
UNITS = 2 + NH


class At:

    def __init__(self, base, reg=None):
        self.base, self.reg = base, reg

    def n(self, per, c=0):
        v = per * self.base + c
        return v if self.reg is None else self.reg * per + v

    @property
    def first(self):
        return self.reg is None and self.base == 0

    @property
    def last(self):
        return self.reg is None and self.base == PAIRS - 1

    def next(self):
        return At(self.base + 1, self.reg)

    def prev(self):
        return At(self.base - 1, self.reg)


class Tally:

    def __init__(self, per_loop):
        self.count, self.per_loop, self.reg, self.start = 0, per_loop, None, 0

    def now(self, more=0):
        n = self.count + more
        return n if self.reg is None else self.reg * self.per_loop + n

    def add(self):
        self.count += 1

    def enter(self, reg):
        self.reg, self.start = reg, self.count

    def leave(self, turns):
        assert self.count - self.start == self.per_loop, (self.count - self.start, self.per_loop)
        self.count, self.reg = self.start + turns * self.per_loop, None


JOBS = {"patch": 1, "qaT": 1, "qbT": 1, "qfT": 1, "vT": 1, "norm": 1, "attnT": 1, "combine": 2,
        "x2T": 2, "logits": 1, "hotT": 1, "ffn2": 1}
JOBS_PER_PAIR = SLOTS * (5 + NG + 1 + 2 + 2 + 1 + 1 + NT)
BANKS = 3
assert JOBS_PER_PAIR % BANKS == 0


def period(i, s):
    last, next_ = ((i.prev(), 1), (i, 1)) if s == 0 else ((i, 0), (i.next(), 0))
    before, after = (i.prev(), s), (i.next(), s)
    has_last = not (i.first and s == 0)
    has_next = not (i.last and s == 1)

    def old(*names):
        return [(name, *last) for name in names] if has_last else []

    def new(*names):
        return [(name, *next_) for name in names] if has_next else []

    def oldest(t):
        return [] if i.first else [("ffn2", *before, t)]

    def newest(*names):
        return [] if i.last else [(name, *after) for name in names]

    between = {
        0: [("keep", i, s)],
        1: ([("norm", *last, 2)] if has_last else []) + oldest(0),
        2: old("attnT"),
        3: oldest(1),
        4: old("combine", "ln2_stats") + new("q"),
        5: old("ln2_apply") + newest("txt", "patch"),
        6: new("qa") + [("pv", i, s, 0)] + old("x2T"),
        7: new("qbT"),
        8: old("logits"),
        9: [("norm", i, s, 0)] + new("qfT") + newest("ln1_stats"),
        10: [("pv", i, s, 1)],
        11: old("hotT") + newest("ln1_apply"),
        12: new("qaT"),
        13: new("vT") + [("norm", i, s, 1)] + newest("cos")}
    for u in range(UNITS):
        yield ("score", i, s, u)
        yield from between.get(u, [])
    if has_last:
        yield ("ffn1", *last, 0)
        yield ("ffn1", *last, 1)
    yield ("pv", i, s, 2)
    if has_last:
        yield ("ffn1", *last, 2)
    yield from oldest(2)


def pair_steps(i):
    for s in range(SLOTS):
        yield from period(i, s)


def first_steps():
    g = At(0)
    for s in range(SLOTS):
        for step in ("txt", "patch", "ln1_stats", "ln1_apply", "cos"):
            yield (step, g, s)
    for step in ("q", "qa", "qbT", "qaT", "qfT", "vT"):
        yield (step, g, 0)


def last_steps():
    g = At(PAIRS - 1)
    yield ("norm", g, 1, 2)
    yield ("ffn2", g, 0, 0)
    yield ("attnT", g, 1)
    yield ("ffn2", g, 0, 1)
    yield ("combine", g, 1)
    yield ("ln2_stats", g, 1)
    yield ("ffn2", g, 0, 2)
    for step in ("ln2_apply", "x2T", "logits", "hotT"):
        yield (step, g, 1)
    for c in range(3):
        yield ("ffn1", g, 1, c)
    for t in range(NT):
        yield ("ffn2", g, 1, t)


def run_steps(eng, mine, tallies):
    def follow(steps):
        for name, i, *where in steps:
            if name in mine:
                mine[name](i, *where)

    follow(first_steps())
    follow(pair_steps(At(0)))
    turns = PAIRS - 2
    with eng.Fori(0, turns) as j:
        for t in tallies:
            t.enter(j)
        follow(pair_steps(At(1, j)))
    for t in tallies:
        t.leave(turns)
    follow(pair_steps(At(PAIRS - 1)))
    follow(last_steps())


def early_fusion_kernel(nc, patches, txt, w_patch, b_patch, pos, theta, w_combine, w_router,
                        b_router, w1, b1, w2, b2, out):
    ctx = ExitStack()
    with ctx:
        def sb(name, shape, dt=f32):
            return ctx.enter_context(nc.sbuf_tensor(name, shape, dt))

        def sem(name):
            return ctx.enter_context(nc.semaphore(name))

        w_patch_sb = sb("w_patch_sb", [128, KP, D])
        pos_sb = sb("pos_sb", [TS, 2, D])
        b_patch_sb = sb("b_patch_sb", [TS, D])
        cos_theta = sb("cos_theta", [TS, NQ])
        w_combine_sb = sb("w_combine_sb", [NQ, D])
        w_router_sb = sb("w_router_sb", [96, 2, RC])
        b_router_sb = sb("b_router_sb", [TS, NE])
        w1_sb = sb("w1_sb", [100, 2, NE * D])
        w2_sb = sb("w2_sb", [128, HC, D])
        b2_sb = sb("b2_sb", [HOT, D])
        b2_parts = sb("b2_parts", [HOT, D], bf16)
        ident = sb("ident", [128, 128])
        ident16 = sb("ident16", [128, 128], f16)
        neg_half = sb("neg_half", [TS, NT])
        half_pi = sb("half_pi", [TS, 1])
        order = sb("order", [TS, NE])
        eps = sb("eps", [TS, NT])
        zero = sb("zero", [TS, 1])
        spare = sb("spare", [1, 1])
        x_sb = sb("x_sb", [128, SLOTS, KP, TI])
        txt_sb = sb("txt_sb", [TS, SLOTS, D])
        h = sb("h", [TS, SLOTS, NT, D])
        stats1 = sb("stats1", [TS, NT, 6])
        moments1 = sb("moments1", [TS, NT, 2])
        rstd1 = sb("rstd1", [TS, SLOTS, NT])
        normed = sb("normed", [TS, NT, NQ])
        turns_sb = sb("turns_sb", [TS, NT, NQ])
        angle = sb("angle", [TS, SLOTS, NT, NQ])
        cos_x = sb("cos_x", [TS, SLOTS, NT, NQ])
        q = sb("q", [TS, SLOTS, NT, NQ])
        q_b = sb("q_b", [TS, SLOTS, NT * NH, 4, DK], f16)
        q_a = sb("q_a", [TS, SLOTS, NT * NH, 4, DK], f16)
        qa_T = sb("qa_T", [128, SLOTS, NG, TK], f16)
        qb_T = sb("qb_T", [128, SLOTS, NG, TK], f16)
        qa_rest = sb("qa_rest", [128, SLOTS, NG, 128], f16)
        q_T = sb("q_T", [NQ, SLOTS, 2 * KC + HG * 32])
        v = sb("v", [128, SLOTS, 2, NH, DK + 1])
        v_rest = sb("v_rest", [128, SLOTS, NG, 128])
        probs = sb("probs", [128, 2, HG, 2, T])
        probs_rest = sb("probs_rest", [128, SLOTS, NG, T])
        o_T = sb("o_T", [128, 2, TP])
        recip = sb("recip", [TS, NT * HG])
        attn = sb("attn", [TS, SLOTS, NT, NQ])
        attn_T = sb("attn_T", [NQ, TP])
        h1 = sb("h1", [TS, SLOTS, NT, D])
        stats2 = sb("stats2", [TS, NT, 6])
        moments2 = sb("moments2", [TS, NT, 2])
        rstd2 = sb("rstd2", [TS, SLOTS, NT])
        x2 = sb("x2", [TS, SLOTS, NT, D])
        resid = sb("resid", [TS, SLOTS, NT, D])
        x2_T = sb("x2_T", [100, 2, SLOTS, TP])
        logit = sb("logit", [TS, NT, NE])
        top = sb("top", [TS, NT])
        ranked = sb("ranked", [TS, NT, NE])
        best = sb("best", [TS, NT])
        onehot = sb("onehot", [TS, NT, 128])
        hot_T = sb("hot_T", [HOT, SLOTS, TP], bf16)
        hidden = sb("hidden", [128, HC, SLOTS, TP])
        o_sb = sb("o_sb", [TS, SLOTS, NT, D])

        pair_ps = [ctx.enter_context(nc.psum_tensor(f"pair_ps{n}", [128, 2, 512], f32)) for n in (0, 1)]
        bank4 = ctx.enter_context(nc.psum_tensor("bank4", [128, 512], f32))
        job_banks = [ctx.enter_context(nc.psum_tensor(f"job_bank{n}", [128, 512], f32)) for n in range(BANKS)]

        consts_loaded = sem("consts_loaded")
        consts_made = sem("consts_made")
        theta_cos = sem("theta_cos")
        consts_ready = sem("consts_ready")
        x_loaded = [sem(f"x_loaded{s}") for s in range(SLOTS)]
        txt_loaded = [sem(f"txt_loaded{s}") for s in range(SLOTS)]
        stored = [sem(f"stored{s}") for s in range(SLOTS)]
        txt_placed, kept = sem("txt_placed"), sem("kept")
        ln1_stats, ln1_rstd, angle_ready, cos_ready = (
            sem("ln1_stats"), sem("ln1_rstd"), sem("angle_ready"), sem("cos_ready"))
        q_split, qa_ready = sem("q_split"), sem("qa_ready")
        scores_done, exp_done = sem("scores_done"), sem("exp_done")
        pv_done, pv_read = sem("pv_done"), sem("pv_read")
        job_done, job_read = sem("job_done"), sem("job_read")
        ln2_stats, ln2_rstd, x2_ready, resid_ready = (
            sem("ln2_stats"), sem("ln2_rstd"), sem("x2_ready"), sem("resid_ready"))
        ffn1_done, gelu_done = sem("ffn1_done"), sem("gelu_done")
        dve_chain, pool_chain = sem("dve_chain"), sem("pool_chain")

        N_CONST_DMAS = 10 + NE + PARTS
        N_MADE = 28

        block = ctx.enter_context(nc.Block())

        @block.sync
        def _(sp):
            for dst, src in ((w_patch_sb[:], w_patch), (pos_sb[:], pos),
                             (b_patch_sb[:], b_patch.partition_broadcast(TS)),
                             (normed[:, 0, :], theta.partition_broadcast(TS)),
                             (w_combine_sb[:], w_combine), 
                             (b_router_sb[:], b_router.partition_broadcast(TS)),
                             (w1_sb[0:96, 0, :], w1[0]), (w1_sb[0:96, 1, :], w1[1]),
                             (w2_sb[:], w2)):
                sp.dma_start(dst, src).then_inc(consts_loaded, 16)

            def load(i, s):
                b = i.n(SLOTS, s)
                if not i.first:
                    sp.wait_ge(ln1_stats, i.n(2, s - 1))
                sp.dma_start(x_sb[:, s], patches[b]).then_inc(x_loaded[s], 16)
                sp.dma_start(txt_sb[0:TX, s, :], txt[b]).then_inc(txt_loaded[s], 16)

            jobs = Tally(JOBS_PER_PAIR)

            def store(i, s, t):
                if t != NT - 1:
                    return
                b = i.n(SLOTS, s)
                sp.wait_ge(job_read, jobs.now())
                sp.dma_start(out[b, 0:TI].rearrange("(t p) d -> p t d", p=TS),
                             o_sb[:, s, 0:2, :]).then_inc(stored[s], 16)
                sp.dma_start(out[b, TI:T], o_sb[0:TX, s, 2, :]).then_inc(stored[s], 16)

            sp.wait_ge(consts_made, N_MADE)
            for e in range(NE):
                sp.dma_start(w1_sb[96 + e:97 + e, 1, e * D:(e + 1) * D], b1[e:e + 1, :]).then_inc(consts_loaded, 16)
            sp.dma_start(w_router_sb[:, :, 0:NE], w_router).then_inc(consts_loaded, 16)
            for k in range(PARTS):
                sp.dma_start(b2_sb[32 * k:32 * k + NE, :], b2).then_inc(consts_loaded, 16)
            for s in range(SLOTS):
                load(At(0), s)
            def load_next(i, s, u):
                if u == 0 and not i.last:
                    load(i.next(), s)

            def count(name):
                def step(i, *where):
                    for _ in range(JOBS[name]):
                        jobs.add()
                    if name == "ffn2":
                        store(i, *where)
                return step

            run_steps(sp, {"score": load_next} | {name: count(name) for name in JOBS}, [jobs])
            for s in range(SLOTS):
                sp.wait_ge(stored[s], 32 * PAIRS + 1)

        @block.gpsimd
        def _(pool):
            made = [0]

            def make(ins):
                made[0] += 1
                ins.then_inc(consts_made, 1)
                pool.wait_ge(consts_made, made[0])

            make(pool.memset(ident[:], 0.0))
            make(pool.memset(ident16[:], 0.0))
            make(pool.memset(neg_half[:], -0.5))
            make(pool.memset(half_pi[:], TWO_PI / 4))
            make(pool.memset(eps[:], EPS))
            make(pool.memset(zero[:], 0.0))
            for e in range(NE):
                make(pool.memset(order[:, e:e + 1], float(NE - e)))
            make(pool.memset(txt_sb[:], 0.0))
            make(pool.memset(w1_sb[96:100, 1, :], CLOSED))
            make(pool.memset(qa_T[:], 0.0))
            make(pool.memset(qa_rest[:], 0.0))
            make(pool.memset(q_T[:], 0.0))
            make(pool.memset(v[:], 1.0))
            make(pool.memset(v_rest[:], 0.0))
            make(pool.memset(o_T[:], 1.0))
            make(pool.memset(onehot[:], 0.0))
            make(pool.memset(b2_sb[:], 0.0))
            make(pool.memset(w_router_sb[:], 0.0))
            make(pool.memset(hidden[:], 0.0))
            for m in (ident, ident16):
                make(pool.affine_select(out=m[:], in_=m[:], compare_op=ALU.not_equal, fill=1.0, base=0,
                                        pattern=[[-1, 128]], channel_multiplier=1))
            for g in range(HG):
                make(pool.memset(v_rest[32 * g:32 * g + KR, :, :, 32 * g + DK:32 * g + DK + 1], 1.0))
            assert made[0] == N_MADE, made

            chain = Tally(2 * SLOTS)

            def link(ins):
                chain.add()
                ins.then_inc(pool_chain, 1)
                pool.wait_ge(pool_chain, chain.now())

            def place_text(i, s):
                pool.wait_ge(txt_loaded[s], i.n(16, 16))
                if not i.first:
                    pool.wait_ge(kept, i.n(2, s - 1))
                pool.tensor_tensor(h[:, s, 2, :], txt_sb[:, s, :], zero[:].to_broadcast([TS, D]), ALU.add).then_inc(txt_placed, 1)

            def keep(i, s):
                pool.wait_ge(angle_ready, i.n(2, s + 1))
                if not i.first:
                    pool.wait_ge(resid_ready, i.n(2, s - 1))
                flat = "p t d -> p (t d)"
                pool.tensor_tensor(h1[:, s].rearrange(flat), h[:, s].rearrange(flat),
                                   zero[:].to_broadcast([TS, NT * D]), ALU.add).then_inc(kept, 1)

            def inverse_deviation(rstd, moments, done, stats, i, s):
                pool.wait_ge(stats, i.n(2, s + 1))
                link(pool.tensor_tensor(rstd[:, s, :], moments[:, :, 1], eps[:], ALU.add))
                pool.tensor_tensor(rstd[:, s, :], rstd[:, s, :], neg_half[:], ALU.pow).then_inc(done, 1)

            def rstd_1(i, s):
                inverse_deviation(rstd1, moments1, ln1_rstd, ln1_stats, i, s)

            def rstd_2(i, s):
                inverse_deviation(rstd2, moments2, ln2_rstd, ln2_stats, i, s)

            def residual(i, s):
                pool.wait_ge(x2_ready, i.n(2, s + 1))
                pool.tensor_tensor(resid[:, s], h1[:, s], x2[:, s], ALU.add).then_inc(resid_ready, 1)

            run_steps(pool, {"txt": place_text, "ln1_stats": rstd_1, "ln2_stats": rstd_2,
                             "keep": keep, "ln2_apply": residual}, [chain])

        @block.scalar
        def _(act):
            act.wait_ge(consts_made, N_MADE)
            act.wait_ge(theta_cos, 1)
            act.activation(cos_theta[:], cos_x[:, 0, 0, :], ACT.Sin, bias=half_pi[:, 0:1],
                           scale=-1.0).then_inc(theta_cos, 1)

            def cosine(i, s):
                act.wait_ge(angle_ready, i.n(2, s + 1))
                act.activation(cos_x[:, s], angle[:, s], ACT.Sin, bias=half_pi[:, 0:1],
                               scale=-1.0).then_inc(cos_ready, 1)

            def exponential(i, s, u):
                n = s * UNITS + u
                act.wait_ge(scores_done, i.n(2 * UNITS, n + 1))
                if u == 0 and not i.first:
                    act.wait_ge(pv_done, i.n(2 * NG, NG * (s - 1)))
                group = NG * s + (u - 2) // HG
                if u >= 2 and (u - 2) % HG == 0 and not (i.first and group < 2):
                    act.wait_ge(pv_done, i.n(2 * NG, group - 1))
                src = pair_ps[(s + u) % 2]
                if u == 0:
                    a, b = probs_rest[:, s, 0:2, :], src[:, :, 0:T]
                elif u == 1:
                    a, b = probs_rest[:, s, 2, :], src[:, 0, 0:T]
                else:
                    j, g = divmod(u - 2, HG)
                    a, b = probs[:, (NG * s + j) % 2, g], src[:, :, 0:T]
                act.activation(a, b, ACT.Exp, scale=DK ** -0.5).then_inc(exp_done, 1)

            def gelu(i, s, c):
                act.wait_ge(ffn1_done, i.n(6, 3 * s + c + 1))
                act.activation(hidden[:, 2 * c:2 * c + 2, s, 0:T], pair_ps[(s + 1 + c) % 2][:, :, 0:T],
                               ACT.Gelu).then_inc(gelu_done, 1)

            def copy_parts(i, s):
                act.wait_ge(q_split, i.n(2, s + 1))
                for part in (0, 1):
                    ins = act.copy(q_a[:, s, :, 2 * part:2 * part + 2, :],
                                   q_b[:, s, :, part, :][:, :, None, :].to_broadcast([TS, NT * NH, 2, DK]))
                ins.then_inc(qa_ready, 1)

            def read_pv(i, s, j):
                n = NG * s + j
                act.wait_ge(pv_done, i.n(2 * NG, n + 1))
                act.copy(o_T[:, n % 2, 0:T], bank4[:, 0:T]).then_inc(pv_read, 1)

            run_steps(act, {"cos": cosine, "qa": copy_parts, "score": exponential, "pv": read_pv,
                            "ffn1": gelu}, [])

        @block.vector
        def _(dve):
            chain = Tally(16 * SLOTS)
            jobs = Tally(JOBS_PER_PAIR)
            read_at = {}

            def link(ins):
                chain.add()
                ins.then_inc(dve_chain, 1)
                dve.wait_ge(dve_chain, chain.now())

            def job_result():
                bank = job_banks[jobs.count % BANKS]
                jobs.add()
                dve.wait_ge(job_done, jobs.now())
                return bank

            def reduce_angle(out, x, tmp, exact_turns):
                link(dve.tensor_scalar(tmp, x, 1 / TWO_PI, ROUND, ALU.mult, ALU.add))
                if exact_turns:
                    link(dve.tensor_scalar(tmp, tmp, ROUND, -TWO_PI, ALU.subtract, ALU.mult))
                    link(dve.tensor_tensor(tmp, tmp, x, ALU.add))
                else:
                    link(dve.tensor_scalar(out, tmp, ROUND, -6.28125, ALU.subtract, ALU.mult))
                    link(dve.tensor_tensor(x, out, x, ALU.add))
                    link(dve.tensor_scalar(tmp, tmp, ROUND, 6.28125 - TWO_PI, ALU.subtract, ALU.mult))
                    link(dve.tensor_tensor(tmp, tmp, x, ALU.add))
                return dve.scalar_tensor_tensor(out, tmp, -1.0, tmp, ALU.mult, ALU.max)

            dve.wait_ge(consts_loaded, 16 * N_CONST_DMAS)
            dve.tensor_tensor(pos_sb[:], pos_sb[:], b_patch_sb[:, None, :].to_broadcast([TS, 2, D]),
                              ALU.add).then_inc(consts_ready, 1)
            reduce_angle(cos_x[:, 0, 0, :], normed[:, 0, :], turns_sb[:, 0, :], False).then_inc(theta_cos, 1)
            dve.wait_ge(theta_cos, 2)
            dve.wait_ge(consts_made, N_MADE)
            dve.tensor_copy(b2_parts[:], b2_sb[:]).then_inc(consts_ready, 1)
            dve.wait_ge(consts_ready, 2)
            for k in range(1, PARTS):
                for q0 in range(k, PARTS):
                    rows = slice(32 * q0, min(32 * q0 + 32, HOT))
                    link(dve.tensor_tensor(b2_sb[rows, :], b2_sb[rows, :], b2_parts[rows, :], ALU.subtract))
                    dve.tensor_copy(b2_parts[rows, :], b2_sb[rows, :]).then_inc(consts_ready, 1)
                    dve.wait_ge(consts_ready, 3 + (k - 1) * (PARTS - 1) + q0 - k)

            for s in range(SLOTS):
                dve.memset(o_sb[:, s], 0.0).then_inc(stored[s], 1)

            def embed(i, s):
                if not i.first:
                    dve.wait_ge(kept, i.n(2, s - 1))
                src = job_result()[0:TS, :].rearrange("p (t c) -> p t c", t=2)[:, :, 0:D]
                dve.tensor_tensor(h[:, s, 0:2, :], src, pos_sb[:], ALU.add).then_inc(job_read, 1)
                read_at["h", s] = jobs.now()

            def moments(x, stats, mom, done):
                for t in range(NT):
                    ins = dve.bn_stats(stats[:, t, :], x[:, t, :])
                link(ins)
                dve.memset(spare[:], 0.0)
                for t in range(NT):
                    ins = dve.bn_aggr(mom[:, t, :], stats[:, t, :])
                ins.then_inc(done, 1)

            def moments_1(i, s):
                dve.wait_ge(job_read, read_at["h", s])
                dve.wait_ge(txt_placed, i.n(2, s + 1))
                moments(h[:, s], stats1, moments1, ln1_stats)

            def angles(i, s):
                dve.wait_ge(ln1_rstd, i.n(2, s + 1))
                for t in range(NT):
                    ins = dve.tensor_scalar(normed[:, t, :], h[:, s, t, 0:NQ], moments1[:, t, 0:1],
                                            rstd1[:, s, t:t + 1], ALU.subtract, ALU.mult)
                link(ins)
                reduce_angle(angle[:, s], normed[:], turns_sb[:], True).then_inc(angle_ready, 1)

            def split_q(i, s):
                dve.wait_ge(cos_ready, i.n(2, s + 1))
                link(dve.tensor_tensor(q[:, s], cos_x[:, s], cos_theta[:, None, :].to_broadcast([TS, NT, NQ]), ALU.mult))
                qv = q[:, s].rearrange("p t (h d) -> p (t h) d", d=DK)
                twice = qv[:, :, None, :].to_broadcast([TS, NT * NH, 2, DK])
                link(dve.tensor_copy(q_b[:, s, :, 0::2, :], twice))
                dve.tensor_tensor(q_b[:, s, :, 1::2, :], twice, q_b[:, s, :, 0::2, :], ALU.subtract).then_inc(q_split, 1)

            def read_parts_T(dst, src):
                return dve.tensor_copy(dst, src[:, 0:NG * TP].rearrange("p (j t) -> p j t", j=NG)[:, :, 0:T])

            def read_qaT(i, s):
                src = job_result()[:, :].bitcast(f16)
                read_parts_T(qa_T[:, s, :, 0:T], src)
                for g in range(HG):
                    part = src[32 * g:32 * g + 32, 0:NG * TP].rearrange("p (j t) -> p j t", j=NG)
                    ins = dve.tensor_copy(qa_rest[32 * g:32 * g + 32, s, :, 32 * g:32 * g + KR], part[:, :, 2 * KC:T])
                ins.then_inc(job_read, 1)

            def read_qbT(i, s):
                read_parts_T(qb_T[:, s, :, 0:T], job_result()[:, :].bitcast(f16)).then_inc(job_read, 1)

            def read_qfT(i, s):
                src = job_result()
                dve.tensor_copy(q_T[:, s, 0:2 * KC], src[0:NQ, 0:2 * KC])
                dve.tensor_copy(q_T[:, s, 2 * KC:].rearrange("p (g t) -> p g t", g=HG)[:, :, 0:KR],
                                src[0:NQ, 2 * KC:T][:, None, :].to_broadcast([NQ, HG, KR])).then_inc(job_read, 1)

            def read_vT(i, s):
                src = job_result()
                dve.tensor_copy(v[:, s, :, :, 0:DK].rearrange("p c h d -> p (c h) d"),
                                src[:, 0:2 * NQ].rearrange("p (x d) -> p x d", d=DK))
                for g in range(HG):
                    part = src[32 * g:32 * g + 32, 2 * NQ:3 * NQ].rearrange("p (j x) -> p j x", j=NG)
                    ins = dve.tensor_copy(v_rest[32 * g:32 * g + 32, s, :, 32 * g:32 * g + DK],
                                          part[:, :, DK * g:DK * g + DK])
                ins.then_inc(job_read, 1)

            def normalise(i, s, j):
                src = job_result()[0:TS, 0:NT * 128].rearrange("p (t g x) -> p t g x", t=NT, g=HG)
                dve.wait_ge(job_read, jobs.now(-1))
                link(dve.reciprocal(recip[:], src[:, :, :, DK].rearrange("p t g -> p (t g)")))
                dst = attn[:, s, :, 32 * j:32 * j + 32].rearrange("p t (g d) -> p t g d", d=DK)
                rv = recip[:].rearrange("p (t g) -> p t g", t=NT)[:, :, :, None].to_broadcast([TS, NT, HG, DK])
                dve.tensor_tensor(dst, src[:, :, :, 0:DK], rv, ALU.mult).then_inc(job_read, 1)

            def read_attnT(i, s):
                dve.tensor_copy(attn_T[:], job_result()[0:NQ, 0:TP]).then_inc(job_read, 1)

            def add_attention(i, s):
                src = job_result()[0:TS, :].rearrange("p (t c) -> p t c", t=2)[:, :, 0:D]
                dve.wait_ge(kept, i.n(2, s + 1))
                dve.tensor_tensor(h1[:, s, 0:2, :], src, h1[:, s, 0:2, :], ALU.add).then_inc(job_read, 1)
                dve.tensor_tensor(h1[:, s, 2, :], job_result()[0:TS, 0:D], h1[:, s, 2, :], ALU.add).then_inc(job_read, 1)
                read_at["h1", s] = jobs.now()

            def moments_2(i, s):
                dve.wait_ge(job_read, read_at["h1", s])
                moments(h1[:, s], stats2, moments2, ln2_stats)

            def norm_2(i, s):
                dve.wait_ge(ln2_rstd, i.n(2, s + 1))
                for t in range(NT):
                    ins = dve.tensor_scalar(x2[:, s, t, :], h1[:, s, t, :], moments2[:, t, 0:1],
                                            rstd2[:, s, t:t + 1], ALU.subtract, ALU.mult)
                ins.then_inc(x2_ready, 1)

            def read_x2T(i, s):
                for c in range(2):
                    dve.tensor_copy(x2_T[0:96, c, s, :], job_result()[0:96, 0:TP]).then_inc(job_read, 1)

            def choose(i, s):
                src = job_result()[0:TS, 0:NT * RC].rearrange("p (t e) -> p t e", e=RC)[:, :, 0:NE]
                link(dve.tensor_tensor(logit[:], src, b_router_sb[:, None, :].to_broadcast([TS, NT, NE]), ALU.add))
                link(dve.tensor_reduce(top[:], logit[:], AX.X, ALU.max))
                link(dve.tensor_tensor(ranked[:], logit[:], top[:, :, None].to_broadcast([TS, NT, NE]), ALU.is_equal))
                link(dve.tensor_tensor(ranked[:], ranked[:], order[:, None, :].to_broadcast([TS, NT, NE]), ALU.mult))
                link(dve.tensor_reduce(best[:], ranked[:], AX.X, ALU.max))
                dve.tensor_tensor(onehot[:].rearrange("p t (k x) -> p t k x", x=32)[:, :, :, 0:NE],
                                  ranked[:, :, None, :].to_broadcast([TS, NT, 4, NE]),
                                  best[:, :, None, None].to_broadcast([TS, NT, 4, NE]),
                                  ALU.is_equal).then_inc(job_read, 1)

            def read_hotT(i, s):
                src = job_result()
                dve.tensor_copy(x2_T[96:100, 1, s, :], src[96:100, 0:TP])
                dve.tensor_copy(hot_T[:, s, :], src[0:HOT, 0:TP]).then_inc(job_read, 1)

            def finish(i, s, t):
                src = job_result()
                if t == 0:
                    dve.wait_ge(resid_ready, i.n(2, s + 1))
                    dve.wait_ge(stored[s], i.n(32, 1))
                dve.tensor_tensor(o_sb[:, s, t, :], src[0:TS, 0:D], resid[:, s, t, :], ALU.add).then_inc(job_read, 1)

            run_steps(dve, {"patch": embed, "ln1_stats": moments_1, "ln1_apply": angles, "q": split_q,
                            "qaT": read_qaT, "qbT": read_qbT, "qfT": read_qfT, "vT": read_vT,
                            "norm": normalise, "attnT": read_attnT,
                            "combine": add_attention, "ln2_stats": moments_2, "ln2_apply": norm_2,
                            "x2T": read_x2T, "logits": choose, "hotT": read_hotT, "ffn2": finish},
                      [chain, jobs])

        @block.tensor
        def _(pe):
            pe.wait_ge(consts_made, N_MADE)
            pe.wait_ge(consts_loaded, 16 * N_CONST_DMAS)
            jobs = Tally(JOBS_PER_PAIR)
            read_at = {}

            def job_bank():
                bank = job_banks[jobs.count % BANKS]
                jobs.add()
                if jobs.reg is not None or jobs.count > BANKS:
                    pe.wait_ge(job_read, jobs.now(-BANKS))
                return bank

            def patch(i, s):
                pe.wait_ge(x_loaded[s], i.n(16, 16))
                bank = job_bank()
                for t in range(2):
                    for k in range(KP):
                        ins = pe.matmul(bank[0:TS, 256 * t:256 * t + D], x_sb[:, s, k, TS * t:TS * t + TS],
                                        w_patch_sb[:, k, :], start=k == 0, stop=k == KP - 1)
                ins.then_inc(job_done, 1)

            def parts_T(src, s):
                dst = job_bank()[:, :].bitcast(f16)
                for j in range(NG):
                    for t in range(NT):
                        at = t * NH + HG * j
                        ins = pe.transpose(dst[:, j * TP + t * TS:j * TP + (t + 1) * TS],
                                           src[:, s, at:at + HG].rearrange("p h x d -> p (h x d)"),
                                           ident16[0:TS, 0:TS])
                ins.then_inc(job_done, 1)

            def qaT(i, s):
                pe.wait_ge(qa_ready, i.n(2, s + 1))
                parts_T(q_a, s)

            def qbT(i, s):
                pe.wait_ge(q_split, i.n(2, s + 1))
                parts_T(q_b, s)

            def qfT(i, s):
                bank = job_bank()
                for t in range(NT):
                    ins = pe.transpose(bank[0:NQ, TS * t:TS * t + TS], q[:, s, t, :], ident[0:TS, 0:TS])
                ins.then_inc(job_done, 1)
                read_at["q_T", s] = jobs.now()

            def vT(i, s):
                bank = job_bank()
                pe.wait_ge(job_read, read_at["q_T", s])
                for c in range(2):
                    pe.transpose(bank[:, NQ * c:NQ * c + NQ], q_T[:, s, KC * c:KC * c + KC], ident[0:NQ, 0:NQ])
                pe.transpose(bank[:, 2 * NQ:3 * NQ], q_T[:, s, 2 * KC:], ident[0:NQ, 0:NQ]).then_inc(job_done, 1)

            def score(i, s, u):
                n = s * UNITS + u
                if u == 0:
                    pe.wait_ge(job_read, jobs.now(0 if i.first else -1))
                if u >= 2:
                    pe.wait_ge(exp_done, i.n(2 * UNITS, n - 1))
                elif not i.first:
                    pe.wait_ge(gelu_done, i.n(6, 3 * s - 4 + u))
                elif s == 1:
                    pe.wait_ge(exp_done, i.n(2 * UNITS, UNITS - u))
                dst = pair_ps[(s + u) % 2]
                if u < 2:
                    for x, j in enumerate((0, 1) if u == 0 else (2,)):
                        ins = pe.matmul(dst[:, x, 0:T], qa_rest[:, s, j, :], qb_T[:, s, j, 0:T], start=True, stop=True)
                else:
                    j, g = divmod(u - 2, HG)
                    for c in range(2):
                        ins = pe.matmul(dst[:, c, 0:T], qa_T[32 * g:32 * g + 32, s, j, KC * c:KC * c + KC],
                                        qb_T[32 * g:32 * g + 32, s, j, 0:T], start=True, stop=True)
                ins.then_inc(scores_done, 1)

            def pv(i, s, j):
                n = NG * s + j
                pe.wait_ge(exp_done, i.n(2 * UNITS, UNITS * s + 2 + HG * (j + 1)))
                if n > 0 or not i.first:
                    pe.wait_ge(pv_read, i.n(2 * NG, n))
                pe.matmul(bank4[:, 0:T], v_rest[:, s, j, :], probs_rest[:, s, j, :], start=True, stop=False)
                for c in range(2):
                    for g in range(HG):
                        ins = pe.matmul(bank4[32 * g:32 * g + DK + 1, 0:T], v[:, s, c, HG * j + g, :],
                                        probs[:, n % 2, g, c, :], start=False, stop=c == 1)
                ins.then_inc(pv_done, 1)

            def norm(i, s, j):
                pe.wait_ge(pv_read, i.n(2 * NG, NG * s + j + 1))
                bank = job_bank()
                for t in range(NT):
                    ins = pe.transpose(bank[0:TS, 128 * t:128 * t + 128],
                                       o_T[:, (NG * s + j) % 2, TS * t:TS * t + TS], ident[:])
                ins.then_inc(job_done, 1)
                read_at["attn", s] = jobs.now()

            def attnT(i, s):
                bank = job_bank()
                pe.wait_ge(job_read, read_at["attn", s])
                for t in range(NT):
                    ins = pe.transpose(bank[0:NQ, TS * t:TS * t + TS], attn[:, s, t, :], ident[0:TS, 0:TS])
                ins.then_inc(job_done, 1)
                read_at["attn_T", s] = jobs.now()

            def combine(i, s):
                for tiles in ((0, 1), (2,)):
                    bank = job_bank()
                    pe.wait_ge(job_read, read_at["attn_T", s])
                    for x, t in enumerate(tiles):
                        ins = pe.matmul(bank[0:TS, 256 * x:256 * x + D], attn_T[:, TS * t:TS * t + TS],
                                        w_combine_sb[:], start=True, stop=True)
                    ins.then_inc(job_done, 1)

            def x2T(i, s):
                pe.wait_ge(x2_ready, i.n(2, s + 1))
                for c in range(2):
                    bank = job_bank()
                    for t in range(NT):
                        ins = pe.transpose(bank[0:96, TS * t:TS * t + TS], x2[:, s, t, 96 * c:96 * c + 96],
                                           ident[0:TS, 0:TS])
                    ins.then_inc(job_done, 1)
                read_at["x2_T", s] = jobs.now()

            def logits(i, s):
                bank = job_bank()
                pe.wait_ge(job_read, read_at["x2_T", s])
                for t in range(NT):
                    for c in range(2):
                        ins = pe.matmul(bank[0:TS, RC * t:RC * t + RC], x2_T[0:96, c, s, TS * t:TS * t + TS],
                                        w_router_sb[:, c, :], start=c == 0, stop=c == 1)
                ins.then_inc(job_done, 1)
                read_at["onehot", s] = jobs.now()

            def hotT(i, s):
                bank = job_bank()
                pe.wait_ge(job_read, read_at["onehot", s])
                for t in range(NT):
                    ins = pe.transpose(bank[0:100, TS * t:TS * t + TS], onehot[:, t, 0:100], ident[0:TS, 0:TS])
                ins.then_inc(job_done, 1)
                read_at["hot_T", s] = jobs.now()

            def ffn1(i, s, c):
                dst = pair_ps[(s + 1 + c) % 2]
                if c == 0:
                    pe.wait_ge(job_read, read_at["hot_T", s])
                if c == 2 or (i.last and s == 1):
                    pe.wait_ge(gelu_done, i.n(6, 3 * s - 1 + c))
                else:
                    pe.wait_ge(exp_done, i.n(2 * UNITS, (s + 2) * UNITS - 1 + c))
                for x in range(2):
                    m = 128 * (2 * c + x)
                    pe.matmul(dst[:, x, 0:T], w1_sb[0:96, 0, m:m + 128], x2_T[0:96, 0, s, 0:T],
                              start=True, stop=False)
                    ins = pe.matmul(dst[:, x, 0:T], w1_sb[0:100, 1, m:m + 128], x2_T[0:100, 1, s, 0:T],
                                    start=False, stop=True)
                ins.then_inc(ffn1_done, 1)

            def ffn2(i, s, t):
                if t == 0:
                    pe.wait_ge(gelu_done, i.n(6, 3 * s + 3))
                dst = job_bank()[0:TS, 0:D]
                tok = slice(TS * t, TS * t + TS)
                for m in range(HC):
                    pe.matmul(dst, hidden[:, m, s, tok], w2_sb[:, m, :], start=m == 0, stop=False)
                pe.matmul(dst, hot_T[:, s, tok], b2_parts[:], start=False, stop=True).then_inc(job_done, 1)

            run_steps(pe, {"patch": patch, "qaT": qaT, "qbT": qbT, "qfT": qfT, "vT": vT, "score": score,
                           "pv": pv, "norm": norm, "attnT": attnT, "combine": combine, "x2T": x2T,
                           "logits": logits, "hotT": hotT, "ffn1": ffn1, "ffn2": ffn2}, [jobs])


def kernel(x, txt, L0_tok_W, L0_tok_b, L0_tok_pos, L0_attn_theta, L0_attn_W_combine, L0_ffn_router_w,
           L0_ffn_router_b, L0_ffn_w1, L0_ffn_b1, L0_ffn_w2, L0_ffn_b2):
    import concourse.bacc as bacc
    from concourse.bass_utils import run_bass_kernel_spmd

    x = np.asarray(x)
    side = x.shape[-1] // 16
    patches = x.reshape(B, 3, side, 16, side, 16).transpose(0, 1, 3, 5, 2, 4).reshape(B, KP, 128, TI)
    arrays = {
        "patches": patches.transpose(0, 2, 1, 3),
        "txt": np.asarray(txt),
        "w_patch": np.asarray(L0_tok_W).T.reshape(KP, 128, D).transpose(1, 0, 2),
        "b_patch": np.asarray(L0_tok_b),
        "pos": np.asarray(L0_tok_pos).reshape(2, TS, D).transpose(1, 0, 2),
        "theta": np.asarray(L0_attn_theta),
        "w_combine": np.asarray(L0_attn_W_combine).T,
        "w_router": np.asarray(L0_ffn_router_w).reshape(2, 96, NE).transpose(1, 0, 2),
        "b_router": np.asarray(L0_ffn_router_b),
        "w1": np.asarray(L0_ffn_w1).transpose(1, 0, 2).reshape(2, 96, NE * D),
        "b1": np.asarray(L0_ffn_b1),
        "w2": np.asarray(L0_ffn_w2).reshape(HC, 128, D).transpose(1, 0, 2),
        "b2": np.asarray(L0_ffn_b2),
    }
    arrays = {k: np.ascontiguousarray(a) for k, a in arrays.items()}
    nc = bacc.Bacc("TRN2", target_bir_lowering=False, num_devices=1)
    aps = {k: nc.dram_tensor(k, a.shape, f32, kind="ExternalInput").ap() for k, a in arrays.items()}
    out = nc.dram_tensor("out", (B, T, D), f32, kind="ExternalOutput").ap()
    early_fusion_kernel(nc, out=out, **aps)
    r = run_bass_kernel_spmd(nc, [arrays], core_ids=[0])
    return r.results[0]["out"]
```
